# Optimizing a Trainium2 kernel written in Bass

```python
import numpy as np
import jax
import jax.numpy as jnp

def _softmax(x, axis=-1):
    return jax.nn.softmax(x, axis=axis)

def _gelu(x):
    return jax.nn.gelu(x, approximate=True)

def _silu(x):
    return jax.nn.silu(x)

def _sigmoid(x):
    return jax.nn.sigmoid(x)

def _layernorm(x, axis=-1, eps=1e-05):
    m = jnp.mean(x, axis=axis, keepdims=True)
    v = jnp.var(x, axis=axis, keepdims=True)
    return (x - m) / jnp.sqrt(v + eps)

def _scatter_add(tgt, idx, src, axis=0):
    return tgt.at[idx].add(src)

def _segment_sum(src, seg, n):
    return jax.ops.segment_sum(src, seg, n)
kernel_name = 'mk_dlrm_tower_d1_rec_r8_e1ff2c'

def setup_inputs(seed: int=0):
    np.random.seed(seed)
    _w = jnp.asarray

    def _rec_inputs():
        import jax
        import jax.numpy as jnp
        _tk = jax.random.key(seed)
        ids = jnp.stack([jax.random.randint(jax.random.fold_in(_tk, 200 + f), (512,), 0, v, jnp.int32) for f, v in enumerate([125000, 12500, 1000, 1000, 1250, 1250, 12500, 12500, 1250, 12500, 1000, 1000, 1000, 12500, 1000, 1000, 1250, 1000, 12500, 1250, 1000, 1000, 1250, 12500, 12500, 1000, 1000])], axis=1)
        tbl_0 = 0.05 * jax.random.normal(jax.random.fold_in(_tk, 500 + 0), (125000, 128), jnp.float32)
        tbl_1 = 0.05 * jax.random.normal(jax.random.fold_in(_tk, 500 + 1), (12500, 128), jnp.float32)
        tbl_2 = 0.05 * jax.random.normal(jax.random.fold_in(_tk, 500 + 2), (1000, 128), jnp.float32)
        tbl_3 = 0.05 * jax.random.normal(jax.random.fold_in(_tk, 500 + 3), (1000, 128), jnp.float32)
        tbl_4 = 0.05 * jax.random.normal(jax.random.fold_in(_tk, 500 + 4), (1250, 128), jnp.float32)
        tbl_5 = 0.05 * jax.random.normal(jax.random.fold_in(_tk, 500 + 5), (1250, 128), jnp.float32)
        tbl_6 = 0.05 * jax.random.normal(jax.random.fold_in(_tk, 500 + 6), (12500, 128), jnp.float32)
        tbl_7 = 0.05 * jax.random.normal(jax.random.fold_in(_tk, 500 + 7), (12500, 128), jnp.float32)
        tbl_8 = 0.05 * jax.random.normal(jax.random.fold_in(_tk, 500 + 8), (1250, 128), jnp.float32)
        tbl_9 = 0.05 * jax.random.normal(jax.random.fold_in(_tk, 500 + 9), (12500, 128), jnp.float32)
        tbl_10 = 0.05 * jax.random.normal(jax.random.fold_in(_tk, 500 + 10), (1000, 128), jnp.float32)
        tbl_11 = 0.05 * jax.random.normal(jax.random.fold_in(_tk, 500 + 11), (1000, 128), jnp.float32)
        tbl_12 = 0.05 * jax.random.normal(jax.random.fold_in(_tk, 500 + 12), (1000, 128), jnp.float32)
        tbl_13 = 0.05 * jax.random.normal(jax.random.fold_in(_tk, 500 + 13), (12500, 128), jnp.float32)
        tbl_14 = 0.05 * jax.random.normal(jax.random.fold_in(_tk, 500 + 14), (1000, 128), jnp.float32)
        tbl_15 = 0.05 * jax.random.normal(jax.random.fold_in(_tk, 500 + 15), (1000, 128), jnp.float32)
        tbl_16 = 0.05 * jax.random.normal(jax.random.fold_in(_tk, 500 + 16), (1250, 128), jnp.float32)
        tbl_17 = 0.05 * jax.random.normal(jax.random.fold_in(_tk, 500 + 17), (1000, 128), jnp.float32)
        tbl_18 = 0.05 * jax.random.normal(jax.random.fold_in(_tk, 500 + 18), (12500, 128), jnp.float32)
        tbl_19 = 0.05 * jax.random.normal(jax.random.fold_in(_tk, 500 + 19), (1250, 128), jnp.float32)
        tbl_20 = 0.05 * jax.random.normal(jax.random.fold_in(_tk, 500 + 20), (1000, 128), jnp.float32)
        tbl_21 = 0.05 * jax.random.normal(jax.random.fold_in(_tk, 500 + 21), (1000, 128), jnp.float32)
        tbl_22 = 0.05 * jax.random.normal(jax.random.fold_in(_tk, 500 + 22), (1250, 128), jnp.float32)
        tbl_23 = 0.05 * jax.random.normal(jax.random.fold_in(_tk, 500 + 23), (12500, 128), jnp.float32)
        tbl_24 = 0.05 * jax.random.normal(jax.random.fold_in(_tk, 500 + 24), (12500, 128), jnp.float32)
        tbl_25 = 0.05 * jax.random.normal(jax.random.fold_in(_tk, 500 + 25), (1000, 128), jnp.float32)
        tbl_26 = 0.05 * jax.random.normal(jax.random.fold_in(_tk, 500 + 26), (1000, 128), jnp.float32)
        _rk = jax.random.fold_in(_tk, 7)
        r_bottom_mlp_out = 4.13588e-05 + 0.999923 * jax.random.normal(jax.random.fold_in(_rk, 101), (512, 128), jnp.float32)
        W_top1 = 0.0405887 * jax.random.normal(jax.random.fold_in(_tk, 801), (607, 512), jnp.float32)
        W_top2 = 0.0441942 * jax.random.normal(jax.random.fold_in(_tk, 802), (512, 256), jnp.float32)
        W_top3 = 0.0625 * jax.random.normal(jax.random.fold_in(_tk, 803), (256, 1), jnp.float32)
        b_top1 = jnp.zeros((512,), jnp.float32)
        b_top2 = jnp.zeros((256,), jnp.float32)
        return (r_bottom_mlp_out, ids, tbl_0, tbl_1, tbl_2, tbl_3, tbl_4, tbl_5, tbl_6, tbl_7, tbl_8, tbl_9, tbl_10, tbl_11, tbl_12, tbl_13, tbl_14, tbl_15, tbl_16, tbl_17, tbl_18, tbl_19, tbl_20, tbl_21, tbl_22, tbl_23, tbl_24, tbl_25, tbl_26, W_top1, b_top1, W_top2, b_top2, W_top3)
    r_bottom_mlp_out, ids, tbl_0, tbl_1, tbl_2, tbl_3, tbl_4, tbl_5, tbl_6, tbl_7, tbl_8, tbl_9, tbl_10, tbl_11, tbl_12, tbl_13, tbl_14, tbl_15, tbl_16, tbl_17, tbl_18, tbl_19, tbl_20, tbl_21, tbl_22, tbl_23, tbl_24, tbl_25, tbl_26, W_top1, b_top1, W_top2, b_top2, W_top3 = _rec_inputs()

    def _L0_rec_setup():
        import jax, jax.numpy as jnp
        import numpy as np
        NUM_FEATURES = 27

        def _tril_indices(F):
            idx = []
            for i in range(F):
                for j in range(i):
                    idx.append(i * F + j)
            return np.asarray(idx, dtype=np.int32)
        TRIL_IDX = _tril_indices(NUM_FEATURES)
        key = jax.random.key(seed)
        k1, k2 = jax.random.split(key)
        B, F, D = (8192, NUM_FEATURES, 128)
        features = jax.random.normal(k1, (B, F, D), dtype=jnp.float32)
        bottom_mlp_out = jax.random.normal(k2, (B, D), dtype=jnp.float32)
        return {'features': features, 'bottom_mlp_out': bottom_mlp_out}
    _L0_rec_all = _L0_rec_setup()
    _L0_rec_in = {k: v for k, v in _L0_rec_all.items() if k in ()}
    del _L0_rec_all
    return {'r_bottom_mlp_out': r_bottom_mlp_out, 'ids': ids, 'tbl_0': tbl_0, 'tbl_1': tbl_1, 'tbl_2': tbl_2, 'tbl_3': tbl_3, 'tbl_4': tbl_4, 'tbl_5': tbl_5, 'tbl_6': tbl_6, 'tbl_7': tbl_7, 'tbl_8': tbl_8, 'tbl_9': tbl_9, 'tbl_10': tbl_10, 'tbl_11': tbl_11, 'tbl_12': tbl_12, 'tbl_13': tbl_13, 'tbl_14': tbl_14, 'tbl_15': tbl_15, 'tbl_16': tbl_16, 'tbl_17': tbl_17, 'tbl_18': tbl_18, 'tbl_19': tbl_19, 'tbl_20': tbl_20, 'tbl_21': tbl_21, 'tbl_22': tbl_22, 'tbl_23': tbl_23, 'tbl_24': tbl_24, 'tbl_25': tbl_25, 'tbl_26': tbl_26, 'W_top1': W_top1, 'b_top1': b_top1, 'W_top2': W_top2, 'b_top2': b_top2, 'W_top3': W_top3}

def reference(r_bottom_mlp_out, ids, tbl_0, tbl_1, tbl_2, tbl_3, tbl_4, tbl_5, tbl_6, tbl_7, tbl_8, tbl_9, tbl_10, tbl_11, tbl_12, tbl_13, tbl_14, tbl_15, tbl_16, tbl_17, tbl_18, tbl_19, tbl_20, tbl_21, tbl_22, tbl_23, tbl_24, tbl_25, tbl_26, W_top1, b_top1, W_top2, b_top2, W_top3):
    import jax
    import jax.numpy as jnp

    def _L0_rec_ref(features, bottom_mlp_out):
        import jax, jax.numpy as jnp
        import numpy as np
        NUM_FEATURES = 27

        def _tril_indices(F):
            idx = []
            for i in range(F):
                for j in range(i):
                    idx.append(i * F + j)
            return np.asarray(idx, dtype=np.int32)
        TRIL_IDX = _tril_indices(NUM_FEATURES)
        B = features.shape[0]
        F = features.shape[1]
        interactions = jnp.einsum('bfd,bgd->bfg', features, features)
        interactions = interactions.reshape(B, F * F)
        x = interactions[:, TRIL_IDX]
        return jnp.concatenate([bottom_mlp_out, x], axis=1)
    e = jnp.stack([tbl_0[ids[:, 0]], tbl_1[ids[:, 1]], tbl_2[ids[:, 2]], tbl_3[ids[:, 3]], tbl_4[ids[:, 4]], tbl_5[ids[:, 5]], tbl_6[ids[:, 6]], tbl_7[ids[:, 7]], tbl_8[ids[:, 8]], tbl_9[ids[:, 9]], tbl_10[ids[:, 10]], tbl_11[ids[:, 11]], tbl_12[ids[:, 12]], tbl_13[ids[:, 13]], tbl_14[ids[:, 14]], tbl_15[ids[:, 15]], tbl_16[ids[:, 16]], tbl_17[ids[:, 17]], tbl_18[ids[:, 18]], tbl_19[ids[:, 19]], tbl_20[ids[:, 20]], tbl_21[ids[:, 21]], tbl_22[ids[:, 22]], tbl_23[ids[:, 23]], tbl_24[ids[:, 24]], tbl_25[ids[:, 25]], tbl_26[ids[:, 26]]], axis=1)
    z = _L0_rec_ref(e, r_bottom_mlp_out)
    z = z.reshape(z.shape[0], -1)
    h = jnp.concatenate([z, r_bottom_mlp_out], axis=1)
    h = jnp.maximum(h @ W_top1 + b_top1, 0.0)
    h = jnp.maximum(h @ W_top2 + b_top2, 0.0)
    y = h @ W_top3
    return y

_drawn_inputs = setup_inputs


def setup_inputs(seed=0):
    import zlib

    import numpy as np

    out = dict(_drawn_inputs(seed))
    spreads = {'b_top1': (0.0, 0.1), 'b_top2': (0.0, 0.1)}
    factors = {'tbl_0': 4.702,
     'tbl_1': 5.223,
     'tbl_2': 4.407,
     'tbl_3': 4.161,
     'tbl_4': 4.783,
     'tbl_5': 4.168,
     'tbl_6': 4.796,
     'tbl_7': 3.91,
     'tbl_8': 4.563,
     'tbl_9': 5.006,
     'tbl_10': 4.309,
     'tbl_11': 4.538,
     'tbl_12': 4.241,
     'tbl_13': 4.299,
     'tbl_14': 4.73,
     'tbl_15': 4.951,
     'tbl_16': 4.781,
     'tbl_17': 5.113,
     'tbl_18': 4.228,
     'tbl_19': 4.802,
     'tbl_20': 4.243,
     'tbl_21': 4.925,
     'tbl_22': 4.71,
     'tbl_23': 4.868,
     'tbl_24': 4.291,
     'tbl_25': 4.907,
     'tbl_26': 4.431}
    for name, (base, spread) in spreads.items():
        noise = np.random.default_rng([zlib.crc32(name.encode()), seed]).standard_normal(out[name].shape)
        drawn = base * np.exp(spread * noise) if base else spread * noise
        out[name] = jnp.asarray(drawn.astype(out[name].dtype))
    for name, factor in factors.items():
        out[name] = (out[name] * factor).astype(out[name].dtype)
    return out
```

```python
from contextlib import ExitStack

import concourse.bass as bass
from concourse import mybir

F32 = mybir.dt.float32
I32 = mybir.dt.int32
ALU = mybir.AluOpType
ACT = mybir.ActivationFunctionType

P = 128
QUAD = 32
PER_GRAM = P // QUAD


def dlrm_tower_kernel(nc, bottom, ids, tables, w1, b1, w2, b2, w3, out):
    B, FEAT = ids.shape
    D = bottom.shape[1]
    N1, N2 = w1.shape[1], w2.shape[1]
    CHUNKS = B // P
    COLS = FEAT - 1
    TILES = -(-COLS // PER_GRAM)
    LAST_ROWS = (COLS - (TILES - 1) * PER_GRAM) * QUAD
    QUADS = -(-FEAT // 4)
    GROUPS = P // PER_GRAM
    GSTEP = 128
    PER_EVAC = 8
    EVACS = GROUPS // PER_EVAC
    K1 = N1 // P
    PAIR_ROWS = FEAT * (FEAT - 1) // 2

    def quad(q):
        return range(4 * q, min(4 * q + 4, FEAT))

    with ExitStack() as ctx:
        def sb(name, shape, dt=F32):
            return ctx.enter_context(nc.sbuf_tensor(name, shape, dt))

        def ps(name, shape):
            return ctx.enter_context(nc.psum_tensor(name, shape, F32))

        def sem(name):
            return ctx.enter_context(nc.semaphore(name))

        ids_sb = sb("ids_sb", [P, CHUNKS * FEAT], I32)
        rows = sb("rows", [P, CHUNKS, FEAT, D])
        ET = sb("ET", [P, 2, P, QUAD])
        Z = sb("Z", [P, 2, TILES, P])
        W1Z = sb("W1Z", [P, TILES, N1])
        W1A = sb("W1A", [P, N1])
        W1B = sb("W1B", [P, N1])
        W2S = sb("W2S", [P, K1, N2])
        W3S = sb("W3S", [P, N2])
        b1_sb = sb("b1_sb", [1, N1])
        b2_sb = sb("b2_sb", [1, N2])
        ones = sb("ones", [1, P])
        ident = sb("ident", [P, P])
        bot = sb("bot", [P, CHUNKS, D])
        botT = sb("botT", [P, CHUNKS, P])
        H1 = sb("H1", [P, N1])
        H1T = sb("H1T", [P, K1, P])
        prod = sb("prod", [P, N2])
        y = sb("y", [P, CHUNKS])

        pT = [ps(f"pT{i}", [P, 4 * P]) for i in range(2)]
        pG = [ps(f"pG{i}", [P, PER_EVAC * GSTEP]) for i in range(2)]
        pH = ps("pH", [P, N1])
        pF = ps("pF", [P, N2])

        ids_in = sem("ids_in")
        bot_in = sem("bot_in")
        weights_in = sem("weights_in")
        w1z_in = sem("w1z_in")
        rows_in = [[sem(f"rows_in_{c}_{q}") for q in range(QUADS)] for c in range(CHUNKS)]
        ident_zero = sem("ident_zero")
        ident_done = sem("ident_done")
        consts_done = sem("consts_done")
        pads_done = sem("pads_done")
        w1z_zeroed = sem("w1z_zeroed")
        bot_transposed = sem("bot_transposed")
        bot_moved = sem("bot_moved")
        transposed = sem("transposed")
        et_act = sem("et_act")
        et_dve = sem("et_dve")
        grams = sem("grams")
        z_act = sem("z_act")
        z_dve = sem("z_dve")
        dense1 = sem("dense1")
        h1_done = sem("h1_done")
        h1_transposed = sem("h1_transposed")
        h1t_done = sem("h1t_done")
        dense2 = sem("dense2")
        y_done = sem("y_done")
        out_done = sem("out_done")

        block = ctx.enter_context(nc.Block())

        quads_of = {0: [q for q in range(QUADS) if q % 2 == 0], 1: [q for q in range(QUADS) if q % 2]}

        def quads_moved(c, q, side):
            return c * len(quads_of[side]) + sum(x <= q for x in quads_of[side])

        @block.sync
        def _(sp):
            sp.dma_start(ids_sb[:, :], ids.rearrange("(p c) f -> p (c f)", c=CHUNKS)).then_inc(ids_in, 16)
            sp.dma_start(bot[:, :, :], bottom.rearrange("(p c) d -> p c d", c=CHUNKS)).then_inc(bot_in, 16)
            sp.dma_start(W1A[:, :], w1[0:D, :]).then_inc(weights_in, 16)
            sp.dma_start(W1B[:, :], w1[D + PAIR_ROWS:D + PAIR_ROWS + D, :]).then_inc(weights_in, 16)
            sp.dma_start(b1_sb[:, :], b1.rearrange("(a n) -> a n", a=1)).then_inc(weights_in, 16)
            sp.dma_start(b2_sb[:, :], b2.rearrange("(a n) -> a n", a=1)).then_inc(weights_in, 16)
            sp.dma_start(W2S[:, :, :], w2.rearrange("(k p) n -> p k n", p=P)).then_inc(weights_in, 16)
            sp.dma_start(W3S[:, :], w3.rearrange("n a -> a n").to_broadcast([P, N2])).then_inc(weights_in, 16)
            sp.wait_ge(w1z_zeroed, 1)
            for f in range(1, FEAT):
                t, r = divmod(f - 1, PER_GRAM)
                at = D + f * (f - 1) // 2
                sp.dma_start(W1Z[QUAD * r:QUAD * r + f, t, :], w1[at:at + f, :]).then_inc(w1z_in, 16)
            sp.wait_ge(y_done, CHUNKS)
            sp.dma_start(out.rearrange("(p c) a -> p (c a)", c=CHUNKS), y[:, :]).then_inc(out_done, 16)
            sp.wait_ge(out_done, 16)

        @block.gpsimd
        def _(pool):
            pool.wait_ge(ids_in, 16)
            for c in range(CHUNKS):
                for f in range(FEAT):
                    pool.indirect_dma_start(
                        out=rows[:, c, f, :], out_offset=None, in_=tables[f][:, :],
                        in_offset=bass.IndirectOffsetOnAxis(ap=ids_sb[:, c * FEAT + f:c * FEAT + f + 1], axis=0),
                    ).then_inc(rows_in[c][f // 4], 16)
                if c == 0:
                    pool.wait_ge(ident_zero, 1)
                    pool.affine_select(out=ident[:, :], in_=ident[:, :], compare_op=ALU.not_equal, fill=1.0,
                                       base=0, pattern=[[-1, P]], channel_multiplier=1).then_inc(ident_done, 1)

        def move_rows(engine_copy, eng, c, q, moved):
            eng.wait_ge(transposed, c * QUADS + q + 1)
            n = len(quad(q))
            engine_copy(ET[:, c % 2, :, 4 * q:4 * q + n].rearrange("d p f -> d f p"),
                        pT[(c * QUADS + q) % 2][:, 0:n * P].rearrange("d (f p) -> d f p", p=P)).then_inc(moved, 1)

        def move_gram(engine_copy, eng, c, u, half, moved):
            eng.wait_ge(grams, c * EVACS + u + 1)
            if c >= 2 and u == 0:
                eng.wait_ge(dense1, c - 1)
            src = pG[(c * EVACS + u) % 2][:, :].rearrange("m (j n) -> m j n", n=GSTEP)
            for s in (2 * half, 2 * half + 1):
                for r in range(PER_GRAM):
                    cols = range(r, COLS, PER_GRAM)
                    last = engine_copy(
                        Z[QUAD * r:QUAD * r + QUAD, c % 2, 0:len(cols), u * PER_EVAC * PER_GRAM + s:(u + 1) * PER_EVAC * PER_GRAM:PER_GRAM],
                        src[QUAD * s:QUAD * s + QUAD, :, COLS * s + r:COLS * s + COLS:PER_GRAM].rearrange("m j t -> m t j"))
            last.then_inc(moved, 1)

        @block.scalar
        def _(act):
            for c in range(CHUNKS):
                for q in quads_of[1]:
                    if c >= 2 and q == 1:
                        act.wait_ge(grams, (c - 1) * EVACS)
                    move_rows(nc.scalar.copy, act, c, q, et_act)
                for u in range(EVACS):
                    move_gram(nc.scalar.copy, act, c, u, 1, z_act)
                act.wait_ge(dense1, c + 1)
                if c:
                    act.wait_ge(h1_transposed, c)
                nc.scalar.activation(H1[:, :], pH[:, :], ACT.Relu).then_inc(h1_done, 1)

        @block.vector
        def _(dve):
            nc.vector.memset(ident[:, :], 0.0).then_inc(ident_zero, 1)
            nc.vector.memset(ones[:, :], 1.0).then_inc(consts_done, 1)
            nc.vector.memset(ET[:, :, :, FEAT:QUAD], 0.0).then_inc(pads_done, 1)
            nc.vector.memset(W1Z[:, :, :], 0.0).then_inc(w1z_zeroed, 1)
            dve.wait_ge(bot_transposed, 1)
            nc.vector.tensor_copy(botT[:, :, :].rearrange("d c p -> d (c p)"), pT[1][:, :]).then_inc(bot_moved, 1)
            for c in range(CHUNKS):
                for q in quads_of[0]:
                    if c >= 2 and q == 0:
                        dve.wait_ge(grams, (c - 1) * EVACS)
                    move_rows(nc.vector.tensor_copy, dve, c, q, et_dve)
                for u in range(EVACS):
                    move_gram(nc.vector.tensor_copy, dve, c, u, 0, z_dve)
                dve.wait_ge(h1_transposed, c + 1)
                nc.vector.tensor_copy(H1T[:, :, :].rearrange("n k p -> n (k p)"), pH[:, :]).then_inc(h1t_done, 1)
                dve.wait_ge(dense2, c + 1)
                if c == 0:
                    dve.wait_ge(weights_in, 6 * 16)
                nc.vector.scalar_tensor_tensor(out=prod[:, :], in0=pF[:, :], scalar=0.0, in1=W3S[:, :],
                                               op0=ALU.max, op1=ALU.mult, accum_out=y[:, c:c + 1]).then_inc(y_done, 1)

        @block.tensor
        def _(pe):
            pe.wait_ge(ident_done, 1)
            pe.wait_ge(bot_in, 16)
            for c in range(CHUNKS):
                last = nc.tensor.transpose(pT[1][:, c * P:(c + 1) * P], bot[:, c, :], ident[:, :])
            last.then_inc(bot_transposed, 1)
            for c in range(CHUNKS):
                for q in range(QUADS):
                    k = c * QUADS + q
                    pe.wait_ge(rows_in[c][q], 16 * len(quad(q)))
                    if k == 1:
                        pe.wait_ge(bot_moved, 1)
                    if k >= 2:
                        cc, qq = divmod(k - 2, QUADS)
                        side = qq % 2
                        pe.wait_ge((et_dve, et_act)[side], quads_moved(cc, qq, side))
                    for i, f in enumerate(quad(q)):
                        last = nc.tensor.transpose(pT[k % 2][:, i * P:(i + 1) * P], rows[:, c, f, :], ident[:, :])
                    last.then_inc(transposed, 1)
                if c == 0:
                    pe.wait_ge(pads_done, 1)
                pe.wait_ge(et_dve, quads_moved(c, QUADS, 0))
                pe.wait_ge(et_act, quads_moved(c, QUADS, 1))
                for u in range(EVACS):
                    k = c * EVACS + u
                    if k >= 2:
                        pe.wait_ge(z_dve, k - 1)
                        pe.wait_ge(z_act, k - 1)
                    for j in range(PER_EVAC):
                        jj = u * PER_EVAC + j
                        last = nc.tensor.matmul(pG[k % 2][:, j * GSTEP:j * GSTEP + PER_GRAM * COLS],
                                                ET[:, c % 2, PER_GRAM * jj:PER_GRAM * (jj + 1), :],
                                                ET[:, c % 2, PER_GRAM * jj:PER_GRAM * (jj + 1), 1:FEAT],
                                                start=True, stop=True)
                    last.then_inc(grams, 1)
                if c == 0:
                    pe.wait_ge(consts_done, 1)
                    pe.wait_ge(weights_in, 6 * 16)
                    pe.wait_ge(w1z_in, 16 * COLS)
                if c:
                    pe.wait_ge(h1t_done, c)
                nc.tensor.matmul(pH[:, :], ones[:, :], b1_sb[:, :], start=True, stop=False)
                nc.tensor.matmul(pH[:, :], botT[:, c, :], W1A[:, :], start=False, stop=False)
                nc.tensor.matmul(pH[:, :], botT[:, c, :], W1B[:, :], start=False, stop=False)
                pe.wait_ge(z_dve, (c + 1) * EVACS)
                pe.wait_ge(z_act, (c + 1) * EVACS)
                for t in range(TILES):
                    k = P if t < TILES - 1 else LAST_ROWS
                    last = nc.tensor.matmul(pH[:, :], Z[0:k, c % 2, t, :], W1Z[0:k, t, :], start=False,
                                            stop=t == TILES - 1)
                last.then_inc(dense1, 1)
                pe.wait_ge(h1_done, c + 1)
                for k in range(K1):
                    last = nc.tensor.transpose(pH[:, k * P:(k + 1) * P], H1[:, k * P:(k + 1) * P], ident[:, :])
                last.then_inc(h1_transposed, 1)
                if c:
                    pe.wait_ge(y_done, c)
                nc.tensor.matmul(pF[:, :], ones[:, :], b2_sb[:, :], start=True, stop=False)
                pe.wait_ge(h1t_done, c + 1)
                for k in range(K1):
                    last = nc.tensor.matmul(pF[:, :], H1T[:, k, :], W2S[:, k, :], start=False, stop=k == K1 - 1)
                last.then_inc(dense2, 1)


def kernel(**inputs):
    import numpy as np
    import concourse.bacc as bacc
    from concourse.bass_utils import run_bass_kernel_spmd

    n_tables = sum(name.startswith("tbl_") for name in inputs)
    names = ["r_bottom_mlp_out", "ids"] + [f"tbl_{i}" for i in range(n_tables)] + ["W_top1", "b_top1", "W_top2", "b_top2", "W_top3"]
    nc = bacc.Bacc("TRN2", target_bir_lowering=False, num_devices=1)
    arrays, aps = {}, {}
    for name in names:
        a = np.ascontiguousarray(inputs[name])
        arrays[f"in_{name}"] = a
        aps[name] = nc.dram_tensor(f"in_{name}", a.shape, mybir.dt.from_np(a.dtype), kind="ExternalInput").ap()
    out = nc.dram_tensor("out_y", (inputs["ids"].shape[0], 1), F32, kind="ExternalOutput").ap()
    dlrm_tower_kernel(nc, aps["r_bottom_mlp_out"], aps["ids"], [aps[f"tbl_{i}"] for i in range(n_tables)],
                      aps["W_top1"], aps["b_top1"], aps["W_top2"], aps["b_top2"], aps["W_top3"], out)
    r = run_bass_kernel_spmd(nc, [arrays], core_ids=[0])
    return r.results[0]["out_y"]
```

```python
from contextlib import ExitStack
from itertools import combinations

import concourse.bass as bass
from concourse import mybir

F32 = mybir.dt.float32
F16 = mybir.dt.float16
BF16 = mybir.dt.bfloat16
I32 = mybir.dt.int32
ALU = mybir.AluOpType
ACT = mybir.ActivationFunctionType

P = 128
QUAD = 32
PER_GRAM = P // QUAD
N_ONE_HOT = 6
TABLE_K = 8
ONE_HOT_ROWS = 2048


def plan_tables(vocab):
    least = min(vocab)
    small = [f for f in range(len(vocab)) if vocab[f] == least and least % TABLE_K == 0 and least < ONE_HOT_ROWS]

    def runs_without(one_hot):
        runs = []
        for f in range(len(vocab)):
            if f in one_hot:
                continue
            if runs and runs[-1][-1] == f - 1 and len(runs[-1]) < 4:
                runs[-1].append(f)
            else:
                runs.append([f])
        return runs

    one_hot = min(combinations(small, N_ONE_HOT), key=lambda fs: len(runs_without(fs)))
    return one_hot, runs_without(one_hot)


def dlrm_tower_kernel(nc, bottom, ids, tables, w1, b1, w2, b2, w3, out):
    B, FEAT = ids.shape
    D = bottom.shape[1]
    N1, N2 = w1.shape[1], w2.shape[1]
    CHUNKS = B // P
    COLS = FEAT - 1
    TILES = -(-COLS // PER_GRAM)
    PACKED = 2
    HALF = QUAD // 2
    WHOLE_TILES = range(2 * PACKED, TILES)
    SHARED_TILES = range(PACKED, 2 * PACKED)
    assert 2 * PACKED * PER_GRAM <= HALF < FEAT
    GROUPS = P // PER_GRAM
    GSTEP = 128
    PER_UNIT = 8
    UNITS = GROUPS // PER_UNIT
    GRAM_ROWS = P - QUAD + COLS
    K1 = N1 // P
    PAIR_ROWS = FEAT * (FEAT - 1) // 2
    BANK = 512

    one_hot, runs = plan_tables([t.shape[0] for t in tables])
    RUNS = len(runs)
    EARLY_RUNS = min(N_ONE_HOT - 1, RUNS)
    slot = {f: i for i, f in enumerate(f for run in runs for f in run)}
    TBL_ROWS = tables[one_hot[0]].shape[0]
    TP = TBL_ROWS // TABLE_K
    TP16 = TP // 16 * 16

    BIAS_ROW = (COLS - PER_GRAM * (TILES - 1)) * QUAD
    assert 0 < BIAS_ROW < P

    def tile_rows(t):
        return P if t < TILES - 1 else BIAS_ROW + 1

    pt_order = [("ids", 0), ("ids", 1)]
    for n in range(N_ONE_HOT):
        pt_order += [("ids", n + 2)] * (n + 2 < N_ONE_HOT) + [(0, n - 1)] * (0 < n <= EARLY_RUNS)
    pt_order += [(c, i) for c in range(CHUNKS) for i in range(RUNS) if (c, i) >= (0, EARLY_RUNS)]

    with ExitStack() as ctx:
        def sb(name, shape, dt=F32):
            return ctx.enter_context(nc.sbuf_tensor(name, shape, dt))

        def ps(name, shape):
            return ctx.enter_context(nc.psum_tensor(name, shape, F32))

        def sem(name):
            return ctx.enter_context(nc.semaphore(name))

        ids_sb = sb("ids_sb", [P, CHUNKS * FEAT], I32)
        ids_h = sb("ids_h", [P, N_ONE_HOT, CHUNKS], F16)
        ids_b = sb("ids_b", [P, 2, B], F16)
        row_i = sb("row_i", [P, TABLE_K], I32)
        row_f = sb("row_f", [P, TABLE_K])
        tbl = sb("tbl", [P, N_ONE_HOT, TABLE_K, D])
        part1 = sb("part1", [P, 2, TABLE_K, D], BF16)
        part2 = sb("part2", [P, 2, TABLE_K, D], BF16)
        part3 = sb("part3", [P, 2, TABLE_K, D], BF16)
        rest = sb("rest", [P, 2, TABLE_K, D])
        hot = sb("hot", [P, 2, TABLE_K, B], BF16)
        rows = sb("rows", [P, 2, len(slot), D])
        ET = sb("ET", [P, CHUNKS, P, QUAD])
        Z = sb("Z", [P, 2, TILES, P])
        W1Z = sb("W1Z", [P, TILES, N1])
        W1A = sb("W1A", [P, N1])
        W1B = sb("W1B", [P, N1])
        W1AB = sb("W1AB", [P, N1])
        W2S = sb("W2S", [P, K1, N2])
        W3S = sb("W3S", [P, N2])
        b2_sb = sb("b2_sb", [P, N2])
        ident = sb("ident", [P, P])
        ident_h = sb("ident_h", [P, P], F16)
        bot = sb("bot", [P, CHUNKS, D])
        botT = sb("botT", [P, CHUNKS, P])
        H1T = sb("H1T", [P, K1, P])
        H2 = sb("H2", [P, N2])
        prod = sb("prod", [P, N2])
        y = sb("y", [P, CHUNKS])

        pT = [ps(f"pT{i}", [P, BANK]) for i in range(2)]
        pG = [ps(f"pG{i}", [P, PER_UNIT * GSTEP]) for i in range(2)]
        pH = ps("pH", [P, K1 * P])
        pF = ps("pF", [P, N2])

        ids_in = sem("ids_in")
        tbl_in = [sem(f"tbl_in_{n}") for n in range(N_ONE_HOT)]
        bot_in = sem("bot_in")
        w1ab_in = sem("w1ab_in")
        weights_in = sem("weights_in")
        w1z_in = sem("w1z_in")
        rows_in = [[sem(f"rows_in_{c}_{i}") for i in range(RUNS)] for c in range(CHUNKS)]
        ident_zero = sem("ident_zero")
        ident_done = sem("ident_done")
        ident_h_done = sem("ident_h_done")
        row_i_done = sem("row_i_done")
        row_f_done = sem("row_f_done")
        ids_h_done = sem("ids_h_done")
        ids_spread = sem("ids_spread")
        ids_b_done = sem("ids_b_done")
        part1_done = sem("part1_done")
        part2_done = sem("part2_done")
        part3_done = sem("part3_done")
        rest_done = sem("rest_done")
        hot_done = sem("hot_done")
        looked_up = sem("looked_up")
        lookup_moved = sem("lookup_moved")
        pads_done = sem("pads_done")
        w1z_zeroed = sem("w1z_zeroed")
        w1ab_done = sem("w1ab_done")
        bot_transposed = sem("bot_transposed")
        bot_moved = sem("bot_moved")
        transposed = sem("transposed")
        et_act = sem("et_act")
        et_dve = sem("et_dve")
        grams = sem("grams")
        z_act = sem("z_act")
        z_dve = sem("z_dve")
        packed = sem("packed")
        dense1 = sem("dense1")
        z_zeroed = sem("z_zeroed")
        ones_done = sem("ones_done")
        h1_done = sem("h1_done")
        dense2 = sem("dense2")
        h2_done = sem("h2_done")
        y_done = sem("y_done")
        out_done = sem("out_done")

        block = ctx.enter_context(nc.Block())

        def mover(i):
            return (et_dve, et_act)[i % 2]

        def moved_until(c, i):
            return c * len(range(i % 2, RUNS, 2)) + i // 2 + 1

        @block.sync
        def _(sp):
            sp.dma_start(ids_sb[:, :], ids.rearrange("(p c) f -> p (c f)", c=CHUNKS)).then_inc(ids_in, 16)
            for n, f in enumerate(one_hot):
                t = tables[f].rearrange("(p k) d -> p k d", k=TABLE_K)
                sp.dma_start(tbl[0:TP16, n, :, :], t[0:TP16, :, :]).then_inc(tbl_in[n], 16)
                sp.dma_start(tbl[TP16:TP, n, :, :], t[TP16:TP, :, :]).then_inc(tbl_in[n], 16)
                if n == 1:
                    sp.dma_start(bot[:, :, :], bottom.rearrange("(p c) d -> p c d", c=CHUNKS)).then_inc(bot_in, 16)
            sp.dma_start(W1A[:, :], w1[0:D, :]).then_inc(w1ab_in, 16)
            sp.dma_start(W1B[:, :], w1[D + PAIR_ROWS:D + PAIR_ROWS + D, :]).then_inc(w1ab_in, 16)
            sp.wait_ge(w1z_zeroed, 1)
            for f in range(1, FEAT):
                t, r = divmod(f - 1, PER_GRAM)
                to, row = (t + PACKED, QUAD * r + HALF) if t < PACKED else (t, QUAD * r)
                at = D + f * (f - 1) // 2
                sp.dma_start(W1Z[row:row + f, to, :], w1[at:at + f, :]).then_inc(w1z_in, 16)
            sp.dma_start(W1Z[BIAS_ROW:BIAS_ROW + 1, TILES - 1, :], b1.rearrange("(a n) -> a n", a=1)).then_inc(w1z_in, 16)
            sp.dma_start(b2_sb[:, :], b2.rearrange("(a n) -> a n", a=1).to_broadcast([P, N2])).then_inc(weights_in, 16)
            sp.dma_start(W2S[:, :, :], w2.rearrange("(k p) n -> p k n", p=P)).then_inc(weights_in, 16)
            sp.dma_start(W3S[:, :], w3.rearrange("n a -> a n").to_broadcast([P, N2])).then_inc(weights_in, 16)
            for c in range(CHUNKS):
                sp.wait_ge(z_dve, (c + 1) * UNITS)
                sp.wait_ge(z_act, (c + 1) * UNITS)
                for r in range(PER_GRAM):
                    sp.dma_start(Z[QUAD * r + HALF:QUAD * (r + 1), c % 2, PACKED:2 * PACKED, :],
                                 Z[QUAD * r:QUAD * r + HALF, c % 2, 0:PACKED, :]).then_inc(packed, 16)
            sp.wait_ge(y_done, CHUNKS)
            sp.dma_start(out.rearrange("(p c) a -> p (c a)", c=CHUNKS), y[:, :]).then_inc(out_done, 16)
            sp.wait_ge(out_done, 16)

        @block.gpsimd
        def _(pool):
            pool.wait_ge(ident_zero, 1)
            pool.affine_select(out=ident[:, :], in_=ident[:, :], compare_op=ALU.not_equal, fill=1.0,
                               base=0, pattern=[[-1, P]], channel_multiplier=1).then_inc(ident_done, 1)
            pool.iota(row_i[:, :], pattern=[[1, TABLE_K]], base=0, channel_multiplier=TABLE_K).then_inc(row_i_done, 1)
            pool.wait_ge(ids_in, 16)
            for c in range(CHUNKS):
                for i, run in enumerate(runs):
                    if c >= 2:
                        pool.wait_ge(transposed, (c - 2) * RUNS + i + 1)
                    for f in run:
                        pool.indirect_dma_start(
                            out=rows[:, c % 2, slot[f], :], out_offset=None, in_=tables[f][:, :],
                            in_offset=bass.IndirectOffsetOnAxis(ap=ids_sb[:, c * FEAT + f:c * FEAT + f + 1], axis=0),
                        ).then_inc(rows_in[c][i], 16)

        def move_run(engine_copy, eng, c, i):
            eng.wait_ge(transposed, c * RUNS + i + 1)
            f0, n = runs[i][0], len(runs[i])
            engine_copy(ET[:, c, :, f0:f0 + n].rearrange("d p f -> d f p"),
                        pT[pt_order.index((c, i)) % 2][:, 0:n * P].rearrange("d (f p) -> d f p", p=P)
                        ).then_inc(mover(i), 1)

        def move_gram(engine_copy, eng, c, u, half, moved):
            eng.wait_ge(grams, c * UNITS + u + 1)
            if c >= 2 and u == 0:
                eng.wait_ge(dense1, c - 1)
            src = pG[(c * UNITS + u) % 2][:, :].rearrange("m (j n) -> m j n", n=GSTEP)
            at = u * PER_UNIT * PER_GRAM
            for s in (2 * half, 2 * half + 1):
                for r in range(PER_GRAM):
                    n = len(range(r, COLS, PER_GRAM))
                    last = engine_copy(
                        Z[QUAD * r:QUAD * r + COLS, c % 2, 0:n, at + s:at + PER_UNIT * PER_GRAM:PER_GRAM],
                        src[QUAD * s:QUAD * s + COLS, :, COLS * s + r:COLS * s + COLS:PER_GRAM].rearrange("m j t -> m t j"))
            last.then_inc(moved, 1)

        @block.scalar
        def _(act):
            def ids_and_part1(n):
                act.wait_ge(ids_spread, n + 1)
                if n >= 2:
                    act.wait_ge(hot_done, (n - 1) * TABLE_K)
                nc.scalar.copy(ids_b[:, n % 2, :], pT[pt_order.index(("ids", n)) % 2][:, :]).then_inc(ids_b_done, 1)
                act.wait_ge(tbl_in[n], 32)
                if n >= 2:
                    act.wait_ge(looked_up, n - 1)
                nc.scalar.copy(part1[0:TP, n % 2, :, :], tbl[0:TP, n, :, :]).then_inc(part1_done, 1)

            def move_lookup(n):
                act.wait_ge(looked_up, n + 1)
                nc.scalar.copy(ET[:, :, :, one_hot[n]].rearrange("d c p -> d (c p)"),
                               pG[n % 2][:, 0:B]).then_inc(lookup_moved, 1)

            ids_and_part1(0)
            for n in range(N_ONE_HOT):
                act.wait_ge(rest_done, n + 1)
                nc.scalar.copy(part2[0:TP, n % 2, :, :], rest[0:TP, n % 2, :, :]).then_inc(part2_done, 1)
                if n + 1 < N_ONE_HOT:
                    ids_and_part1(n + 1)
                if n:
                    move_lookup(n - 1)
                if n >= 2 and (n - 2) % 2 == 1 and n - 2 < EARLY_RUNS:
                    move_run(nc.scalar.copy, act, 0, n - 2)
                if n == 0:
                    nc.scalar.memzero(W1Z[:, PACKED:TILES, :]).then_inc(w1z_zeroed, 1)
                if n == 1:
                    nc.scalar.memzero(ET[:, :, :, FEAT:QUAD]).then_inc(pads_done, 1)
            move_lookup(N_ONE_HOT - 1)

            def relu_h1(c):
                act.wait_ge(dense1, c + 1)
                nc.scalar.activation(H1T[:, :, :].rearrange("n k p -> n (k p)"), pH[:, :], ACT.Relu).then_inc(h1_done, 1)

            def runs_of(c, first, end):
                for i in range(first, end):
                    if i % 2 == 1:
                        move_run(nc.scalar.copy, act, c, i)

            runs_of(0, max(N_ONE_HOT - 2, 0), RUNS)
            for c in range(CHUNKS):
                if c == 0:
                    act.wait_ge(z_zeroed, 1)
                for u in range(UNITS):
                    move_gram(nc.scalar.copy, act, c, u, 1, z_act)
                ahead = min(TILES - PACKED - 1, RUNS - 1)
                if c + 1 < CHUNKS:
                    runs_of(c + 1, 0, ahead)
                relu_h1(c)
                if c + 1 < CHUNKS:
                    runs_of(c + 1, ahead, RUNS)

        @block.vector
        def _(dve):
            nc.vector.memset(ident[:, :], 0.0).then_inc(ident_zero, 1)
            nc.vector.memset(Z[:, :, :, :], 0.0).then_inc(z_zeroed, 1)
            dve.wait_ge(z_zeroed, 1)
            nc.vector.memset(Z[BIAS_ROW:BIAS_ROW + 1, :, TILES - 1, :], 1.0).then_inc(ones_done, 1)
            dve.wait_ge(row_i_done, 1)
            nc.vector.tensor_copy(row_f[:, :], row_i[:, :]).then_inc(row_f_done, 1)
            dve.wait_ge(ident_done, 1)
            nc.vector.tensor_copy(ident_h[:, :], ident[:, :]).then_inc(ident_h_done, 1)
            dve.wait_ge(ids_in, 16)
            ids_cf = ids_sb[:, :].rearrange("p (c f) -> p c f", f=FEAT)
            for n, f in enumerate(one_hot):
                nc.vector.tensor_copy(ids_h[:, n, :], ids_cf[:, :, f]).then_inc(ids_h_done, 1)
            dve.wait_ge(row_f_done, 1)
            for n in range(N_ONE_HOT):
                dve.wait_ge(ids_b_done, n + 1)
                if n >= 2:
                    dve.wait_ge(looked_up, n - 1)
                for k in range(TABLE_K):
                    nc.vector.tensor_scalar(hot[0:TP, n % 2, k, :], ids_b[0:TP, n % 2, :], row_f[0:TP, k:k + 1],
                                            None, ALU.is_equal).then_inc(hot_done, 1)
                dve.wait_ge(part1_done, n + 1)
                if n >= 2:
                    dve.wait_ge(part2_done, n - 1)
                nc.vector.tensor_tensor(rest[0:TP, n % 2, :, :], tbl[0:TP, n, :, :], part1[0:TP, n % 2, :, :],
                                        ALU.subtract).then_inc(rest_done, 1)
                if n == 3:
                    dve.wait_ge(w1ab_in, 32)
                    nc.vector.tensor_tensor(W1AB[:, :], W1A[:, :], W1B[:, :], ALU.add).then_inc(w1ab_done, 1)
                if n == 2:
                    dve.wait_ge(bot_transposed, 1)
                    nc.vector.tensor_copy(botT[:, :, :].rearrange("d c p -> d (c p)"), pH[:, :]).then_inc(bot_moved, 1)
                dve.wait_ge(part2_done, n + 1)
                dve.wait_ge(rest_done, n + 1)
                nc.vector.tensor_tensor(part3[0:TP, n % 2, :, :], rest[0:TP, n % 2, :, :], part2[0:TP, n % 2, :, :],
                                        ALU.subtract).then_inc(part3_done, 1)
                if n >= 2 and (n - 2) % 2 == 0 and n - 2 < EARLY_RUNS:
                    move_run(nc.vector.tensor_copy, dve, 0, n - 2)

            def dense3(c):
                dve.wait_ge(dense2, c + 1)
                if c == 0:
                    dve.wait_ge(weights_in, 3 * 16)
                if c:
                    dve.wait_ge(y_done, c)
                nc.vector.tensor_tensor(H2[:, :], pF[:, :], b2_sb[:, :], ALU.add).then_inc(h2_done, 1)
                dve.wait_ge(h2_done, c + 1)
                nc.vector.scalar_tensor_tensor(out=prod[:, :], in0=H2[:, :], scalar=0.0, in1=W3S[:, :],
                                               op0=ALU.max, op1=ALU.mult, accum_out=y[:, c:c + 1]).then_inc(y_done, 1)

            def runs_of(c, first, end):
                for i in range(first, end):
                    if i % 2 == 0:
                        move_run(nc.vector.tensor_copy, dve, c, i)

            runs_of(0, max(N_ONE_HOT - 2, 0), RUNS)
            for c in range(CHUNKS):
                for u in range(UNITS):
                    move_gram(nc.vector.tensor_copy, dve, c, u, 0, z_dve)
                if 0 < c < CHUNKS - 1:
                    dense3(c - 1)
                if c + 1 < CHUNKS:
                    runs_of(c + 1, 0, RUNS)
                if c == CHUNKS - 2:
                    dense3(c)
            dense3(CHUNKS - 1)

        @block.tensor
        def _(pe):
            def free_pt(use):
                k = pt_order.index(use)
                if k >= 2:
                    before = pt_order[k - 2]
                    if before[0] == "ids":
                        pe.wait_ge(ids_b_done, before[1] + 1)
                    else:
                        pe.wait_ge(mover(before[1]), moved_until(*before))
                return pT[k % 2]

            def spread_ids(n):
                pe.wait_ge(ids_h_done, n + 1)
                bank = free_pt(("ids", n))
                for c in range(CHUNKS):
                    last = nc.tensor.matmul(bank[:, c * P:(c + 1) * P], ids_h[:, n, c:c + 1].to_broadcast([P, P]),
                                            ident_h[:, :], start=True, stop=True)
                last.then_inc(ids_spread, 1)

            def transpose_run(c, i):
                pe.wait_ge(rows_in[c][i], 16 * len(runs[i]))
                bank = free_pt((c, i))
                for x, f in enumerate(runs[i]):
                    last = nc.tensor.transpose(bank[:, x * P:(x + 1) * P], rows[:, c % 2, slot[f], :], ident[:, :])
                last.then_inc(transposed, 1)

            def dense_layer2(c):
                pe.wait_ge(h1_done, c + 1)
                if c:
                    pe.wait_ge(h2_done, c)
                for k in range(K1):
                    last = nc.tensor.matmul(pF[:, :], H1T[:, k, :], W2S[:, k, :], start=k == 0, stop=k == K1 - 1)
                last.then_inc(dense2, 1)

            pe.wait_ge(ident_h_done, 1)
            spread_ids(0)
            spread_ids(1)
            for n in range(N_ONE_HOT):
                if n == 1:
                    pe.wait_ge(bot_in, 16)
                    for c in range(CHUNKS):
                        last = nc.tensor.transpose(pH[:, c * P:(c + 1) * P], bot[:, c, :], ident[:, :])
                    last.then_inc(bot_transposed, 1)
                if n >= 2:
                    pe.wait_ge(lookup_moved, n - 1)
                for x, (part, done) in enumerate(((part1, part1_done), (part2, part2_done), (part3, part3_done))):
                    pe.wait_ge(done, n + 1)
                    for k in range(TABLE_K):
                        if x == 0:
                            pe.wait_ge(hot_done, n * TABLE_K + k + 1)
                        last = nc.tensor.matmul(pG[n % 2][:, 0:B], part[0:TP, n % 2, k, :], hot[0:TP, n % 2, k, :],
                                                start=x == 0 and k == 0, stop=x == 2 and k == TABLE_K - 1)
                last.then_inc(looked_up, 1)
                if n + 2 < N_ONE_HOT:
                    spread_ids(n + 2)
                if 0 < n <= EARLY_RUNS:
                    transpose_run(0, n - 1)
            for i in range(EARLY_RUNS, RUNS):
                transpose_run(0, i)
            pe.wait_ge(lookup_moved, N_ONE_HOT)
            pe.wait_ge(pads_done, 1)

            def dense_layer1(weights, acts, first=False, last=False):
                for k in range(K1):
                    done = nc.tensor.matmul(pH[:, k * P:(k + 1) * P], weights[:, k * P:(k + 1) * P], acts,
                                            start=first and k == 0, stop=last, skip_group_check=True)
                return done

            def begin_chunk(c):
                if c:
                    dense_layer2(c - 1)
                else:
                    pe.wait_ge(bot_moved, 1)
                    pe.wait_ge(w1ab_done, 1)
                    pe.wait_ge(weights_in, 3 * 16)
                dense_layer1(W1AB, botT[:, c, :], first=True)

            for c in range(CHUNKS):
                if c == CHUNKS - 1:
                    begin_chunk(c)
                for i in range(max(RUNS - 2, 0), RUNS):
                    pe.wait_ge(mover(i), moved_until(c, i))
                for u in range(UNITS):
                    k = c * UNITS + u
                    if k >= 2:
                        pe.wait_ge(z_dve, k - 1)
                        pe.wait_ge(z_act, k - 1)
                    for j in range(PER_UNIT):
                        s0 = PER_GRAM * (u * PER_UNIT + j)
                        four = ET[:, c, s0:s0 + PER_GRAM, :]
                        last = nc.tensor.matmul(pG[k % 2][0:GRAM_ROWS, j * GSTEP:j * GSTEP + PER_GRAM * COLS],
                                                four.rearrange("d s f -> d (s f)")[:, 0:GRAM_ROWS], four[:, :, 1:FEAT],
                                                start=True, stop=True)
                    last.then_inc(grams, 1)
                if c < CHUNKS - 1:
                    begin_chunk(c)
                if c == 0:
                    pe.wait_ge(ones_done, 1)
                    pe.wait_ge(w1z_in, 16 * (COLS + 1))
                pe.wait_ge(z_dve, (c + 1) * UNITS)
                pe.wait_ge(z_act, (c + 1) * UNITS)
                tiles = [*WHOLE_TILES, *SHARED_TILES]
                ahead = min(len(tiles) - 1, RUNS - 1)
                for x, t in enumerate(tiles):
                    if t == SHARED_TILES[0]:
                        pe.wait_ge(packed, 16 * PER_GRAM * (c + 1))
                    k = tile_rows(t)
                    done = dense_layer1(W1Z[0:k, t, :], Z[0:k, c % 2, t, :], last=t == tiles[-1])
                    if c + 1 < CHUNKS and x < ahead:
                        transpose_run(c + 1, x)
                done.then_inc(dense1, 1)
                if c + 1 < CHUNKS:
                    for i in range(ahead, RUNS):
                        transpose_run(c + 1, i)
            dense_layer2(CHUNKS - 1)


def kernel(**inputs):
    import numpy as np
    import concourse.bacc as bacc
    from concourse.bass_utils import run_bass_kernel_spmd

    n_tables = sum(name.startswith("tbl_") for name in inputs)
    names = ["r_bottom_mlp_out", "ids"] + [f"tbl_{i}" for i in range(n_tables)] + ["W_top1", "b_top1", "W_top2", "b_top2", "W_top3"]
    nc = bacc.Bacc("TRN2", target_bir_lowering=False, num_devices=1)
    arrays, aps = {}, {}
    for name in names:
        a = np.ascontiguousarray(inputs[name])
        arrays[f"in_{name}"] = a
        aps[name] = nc.dram_tensor(f"in_{name}", a.shape, mybir.dt.from_np(a.dtype), kind="ExternalInput").ap()
    out = nc.dram_tensor("out_y", (inputs["ids"].shape[0], 1), F32, kind="ExternalOutput").ap()
    dlrm_tower_kernel(nc, aps["r_bottom_mlp_out"], aps["ids"], [aps[f"tbl_{i}"] for i in range(n_tables)],
                      aps["W_top1"], aps["b_top1"], aps["W_top2"], aps["b_top2"], aps["W_top3"], out)
    r = run_bass_kernel_spmd(nc, [arrays], core_ids=[0])
    return r.results[0]["out_y"]
```

```python
from contextlib import ExitStack
from itertools import combinations

import concourse.bass as bass
from concourse import mybir

F32 = mybir.dt.float32
F16 = mybir.dt.float16
F32R = mybir.dt.float32r
I32 = mybir.dt.int32
ALU = mybir.AluOpType
ACT = mybir.ActivationFunctionType

P = 128
QUAD = 32
PER_GRAM = P // QUAD
N_ONE_HOT = 8
WARM_UP = (20, 14)
TABLE_RING = 5
TABLE_K = 8
ACT_BLOCK = TABLE_K - 1
ONE_HOT_ROWS = 2048


def plan_tables(vocab):
    least = min(vocab)
    small = [f for f in range(len(vocab)) if vocab[f] == least and least % TABLE_K == 0 and least < ONE_HOT_ROWS]

    def runs_without(one_hot):
        runs = []
        for f in range(len(vocab)):
            if f in one_hot:
                continue
            if runs and runs[-1][-1] == f - 1 and len(runs[-1]) < 4:
                runs[-1].append(f)
            else:
                runs.append([f])
        return runs

    one_hot = min(combinations(small, N_ONE_HOT), key=lambda fs: len(runs_without(fs)))
    return one_hot, runs_without(one_hot)


def dlrm_tower_kernel(nc, bottom, ids, tables, w1, b1, w2, b2, w3, out):
    B, FEAT = ids.shape
    D = bottom.shape[1]
    N1, N2 = w1.shape[1], w2.shape[1]
    CHUNKS = B // P
    COLS = FEAT - 1
    TILES = -(-COLS // PER_GRAM)
    STAGED = TILES // 2
    LONG = COLS % PER_GRAM or PER_GRAM
    FIRST_TILE = [int(r >= LONG) for r in range(PER_GRAM)]
    FREE_ROW = STAGED * PER_GRAM + STAGED * PER_GRAM - LONG
    FREE = QUAD - FREE_ROW

    def place(f):
        t, r = divmod(f - 1, PER_GRAM)
        return r, FIRST_TILE[r] + t

    for f in range(1, FEAT):
        if place(f)[1] < STAGED:
            assert f <= FREE and f + STAGED * PER_GRAM <= FREE_ROW
    assert 2 * STAGED < TILES and COLS < QUAD
    GROUPS = P // PER_GRAM
    GSTEP = 128
    PER_UNIT = 8
    UNITS = GROUPS // PER_UNIT
    GRAM_ROWS = P - QUAD + COLS
    K1 = N1 // P
    PAIR_ROWS = FEAT * (FEAT - 1) // 2
    BANK = 512

    one_hot, all_runs = plan_tables([t.shape[0] for t in tables])
    LAST = CHUNKS - 1
    runs = [list(all_runs) for c in range(CHUNKS)]
    end_run = runs[LAST].pop()
    runs[LAST] += [end_run[:-1], end_run[-1:]]
    RUNS = [len(runs[c]) for c in range(CHUNKS)]
    LATE_RUNS = [2 * (c == LAST) for c in range(CHUNKS)]
    EARLY_RUNS = min(N_ONE_HOT - 1, RUNS[0])
    DVE_LATER = max(N_ONE_HOT - 4, 0)
    slot = {f: i for i, f in enumerate(f for run in runs[0] for f in run)}
    TBL_ROWS = tables[one_hot[0]].shape[0]
    TP = TBL_ROWS // TABLE_K
    TP16 = TP // 16 * 16

    BIAS_ROW = P - 1

    pt_order = [("ids", 0), ("ids", 1)]
    for n in range(N_ONE_HOT):
        pt_order += [("ids", n + 2)] * (n + 2 < N_ONE_HOT) + [(0, n - 1)] * (0 < n <= EARLY_RUNS)
    pt_order += [(c, i) for c in range(CHUNKS) for i in range(RUNS[c]) if (c, i) >= (0, EARLY_RUNS)]

    with ExitStack() as ctx:
        def sb(name, shape, dt=F32):
            return ctx.enter_context(nc.sbuf_tensor(name, shape, dt))

        def ps(name, shape):
            return ctx.enter_context(nc.psum_tensor(name, shape, F32))

        def sem(name):
            return ctx.enter_context(nc.semaphore(name))

        ids_sb = sb("ids_sb", [P, CHUNKS * FEAT], I32)
        ids_h = sb("ids_h", [P, N_ONE_HOT, CHUNKS], F16)
        ids_b = sb("ids_b", [P, 2, B])
        row_i = sb("row_i", [P, TABLE_K], I32)
        row_f = sb("row_f", [P, TABLE_K])
        tbl = sb("tbl", [P, TABLE_RING, TABLE_K, D])
        high = sb("high", [P, 2, TABLE_K, D], F32R)
        low = sb("low", [P, 2, TABLE_K, D], F32R)
        hot = sb("hot", [P, 2, TABLE_K, B], F32R)
        away = sb("away", [P, B])
        rows = sb("rows", [P, 2, len(slot), D])
        ET = sb("ET", [P, CHUNKS, P, QUAD])
        Z = sb("Z", [P, 2, TILES, P])
        W1Z = sb("W1Z", [P, TILES - STAGED, N1])
        W1A = sb("W1A", [P, N1])
        W1B = sb("W1B", [P, N1])
        W1AB = sb("W1AB", [P, N1])
        W2S = sb("W2S", [P, K1, N2])
        W3S = sb("W3S", [P, N2])
        b2_sb = sb("b2_sb", [P, N2])
        ident = sb("ident", [P, P])
        ident_h = sb("ident_h", [P, P], F16)
        ones = sb("ones", [1, P])
        warm = sb("warm", [P, P], F16)
        bot = sb("bot", [P, CHUNKS, D])
        botT = sb("botT", [P, CHUNKS, P])
        H1T = sb("H1T", [P, K1, P])
        H2 = sb("H2", [P, N2])
        prod = sb("prod", [P, N2])
        y = sb("y", [P, CHUNKS])

        pT = [ps(f"pT{i}", [P, BANK]) for i in range(2)]
        pG = [ps(f"pG{i}", [P, PER_UNIT * GSTEP]) for i in range(2)]
        pH = ps("pH", [P, K1 * P])
        pF = ps("pF", [P, N2])
        spare_use = (LAST, RUNS[LAST] - 2)
        pH_last = pT[pt_order.index(spare_use) % 2]

        ids_in = sem("ids_in")
        tbl_in = [sem(f"tbl_in_{n}") for n in range(N_ONE_HOT)]
        bot_in = sem("bot_in")
        w1ab_in = sem("w1ab_in")
        weights_in = sem("weights_in")
        w1z_in = sem("w1z_in")
        rows_in = [[sem(f"rows_in_{c}_{i}") for i in range(RUNS[c])] for c in range(CHUNKS)]
        ident_zero = sem("ident_zero")
        ident_done = sem("ident_done")
        ident_h_done = sem("ident_h_done")
        row_i_done = sem("row_i_done")
        row_f_done = sem("row_f_done")
        ids_h_done = sem("ids_h_done")
        ids_spread = sem("ids_spread")
        ids_b_done = sem("ids_b_done")
        high_done = sem("high_done")
        low_done = sem("low_done")
        hot_done = sem("hot_done")
        away_done = sem("away_done")
        hot_act_done = sem("hot_act_done")
        looked_up = sem("looked_up")
        lookup_moved = sem("lookup_moved")
        pads_done = sem("pads_done")
        w1z_zeroed = sem("w1z_zeroed")
        w1ab_done = sem("w1ab_done")
        bot_transposed = sem("bot_transposed")
        bot_moved = sem("bot_moved")
        transposed = sem("transposed")
        et_act = sem("et_act")
        et_dve = sem("et_dve")
        grams = sem("grams")
        z_act = sem("z_act")
        z_dve = sem("z_dve")
        packed_long = sem("packed_long")
        packed_short = sem("packed_short")
        packed_pool = sem("packed_pool")
        warm_done = sem("warm_done")
        dense1 = sem("dense1")
        z_zeroed = sem("z_zeroed")
        ones_done = sem("ones_done")
        h1_done = sem("h1_done")
        dense2 = sem("dense2")
        h2_done = sem("h2_done")
        y_done = sem("y_done")
        out_done = sem("out_done")

        block = ctx.enter_context(nc.Block())

        def mover(i):
            return (et_dve, et_act)[i % 2]

        def moved_until(c, i):
            return sum(len(range(i % 2, RUNS[b], 2)) for b in range(c)) + i // 2 + 1

        def transposed_until(c, i):
            return sum(RUNS[:c]) + i + 1

        def pack(eng, c, r):
            return eng.dma_start(Z[QUAD * r + FREE_ROW:QUAD * (r + 1), c % 2, STAGED + FIRST_TILE[r]:2 * STAGED, :],
                                 Z[QUAD * r:QUAD * r + FREE, c % 2, FIRST_TILE[r]:STAGED, :])

        @block.sync
        def _(sp):
            sp.dma_start(ids_sb[:, :], ids.rearrange("(p c) f -> p (c f)", c=CHUNKS)).then_inc(ids_in, 16)
            for n, f in enumerate(one_hot):
                if n >= TABLE_RING:
                    sp.wait_ge(low_done, n - TABLE_RING + 1)
                t = tables[f].rearrange("(p k) d -> p k d", k=TABLE_K)
                sp.dma_start(tbl[0:TP16, n % TABLE_RING, :, :], t[0:TP16, :, :]).then_inc(tbl_in[n], 16)
                sp.dma_start(tbl[TP16:TP, n % TABLE_RING, :, :], t[TP16:TP, :, :]).then_inc(tbl_in[n], 16)
                if n == 1:
                    sp.dma_start(bot[:, :, :], bottom.rearrange("(p c) d -> p c d", c=CHUNKS)).then_inc(bot_in, 16)
            sp.dma_start(W1A[:, :], w1[0:D, :]).then_inc(w1ab_in, 16)
            sp.dma_start(W1B[:, :], w1[D + PAIR_ROWS:D + PAIR_ROWS + D, :]).then_inc(w1ab_in, 16)
            sp.wait_ge(w1z_zeroed, TILES - STAGED)
            for f in range(1, FEAT):
                r, t = place(f)
                to, row = (t, QUAD * r + FREE_ROW) if t < STAGED else (t - STAGED, QUAD * r)
                at = D + f * (f - 1) // 2
                sp.dma_start(W1Z[row:row + f, to, :], w1[at:at + f, :]).then_inc(w1z_in, 16)
            sp.dma_start(W1Z[BIAS_ROW:BIAS_ROW + 1, TILES - 1 - STAGED, :], b1.rearrange("(a n) -> a n", a=1)).then_inc(w1z_in, 16)
            sp.dma_start(b2_sb[:, :], b2.rearrange("(a n) -> a n", a=1).to_broadcast([P, N2])).then_inc(weights_in, 16)
            sp.dma_start(W2S[:, :, :], w2.rearrange("(k p) n -> p k n", p=P)).then_inc(weights_in, 16)
            sp.dma_start(W3S[:, :], w3.rearrange("n a -> a n").to_broadcast([P, N2])).then_inc(weights_in, 16)
            for c in range(CHUNKS):
                sp.wait_ge(z_dve, (c + 1) * UNITS)
                sp.wait_ge(z_act, (c + 1) * UNITS)
                for r in [r for r in range(PER_GRAM) if (c, r) != (LAST, LONG - 1)]:
                    pack(sp, c, r).then_inc(packed_long if r < LONG else packed_short, 16)
            sp.wait_ge(y_done, CHUNKS)
            sp.dma_start(out.rearrange("(p c) a -> p (c a)", c=CHUNKS), y[:, :]).then_inc(out_done, 16)
            sp.wait_ge(out_done, 16)

        @block.gpsimd
        def _(pool):
            pool.wait_ge(ident_zero, 1)
            pool.affine_select(out=ident[:, :], in_=ident[:, :], compare_op=ALU.not_equal, fill=1.0,
                               base=0, pattern=[[-1, P]], channel_multiplier=1).then_inc(ident_done, 1)
            pool.iota(row_i[:, :], pattern=[[1, TABLE_K]], base=0, channel_multiplier=TABLE_K).then_inc(row_i_done, 1)
            pool.wait_ge(ids_in, 16)
            for c in range(CHUNKS):
                for i, run in enumerate(runs[c]):
                    if c >= 2:
                        pool.wait_ge(transposed, transposed_until(c - 2, max(
                            j for j, before in enumerate(runs[c - 2]) if set(before) & set(run))))
                    for f in run:
                        pool.indirect_dma_start(
                            out=rows[:, c % 2, slot[f], :], out_offset=None, in_=tables[f][:, :],
                            in_offset=bass.IndirectOffsetOnAxis(ap=ids_sb[:, c * FEAT + f:c * FEAT + f + 1], axis=0),
                        ).then_inc(rows_in[c][i], 16)
            pool.wait_ge(z_dve, CHUNKS * UNITS)
            pool.wait_ge(z_act, CHUNKS * UNITS)
            pack(pool, LAST, LONG - 1).then_inc(packed_pool, 16)

        def move_run(engine_copy, eng, c, i):
            eng.wait_ge(transposed, transposed_until(c, i))
            f0, n = runs[c][i][0], len(runs[c][i])
            engine_copy(ET[:, c, :, f0:f0 + n].rearrange("d p f -> d f p"),
                        pT[pt_order.index((c, i)) % 2][:, 0:n * P].rearrange("d (f p) -> d f p", p=P)
                        ).then_inc(mover(i), 1)

        def move_gram(engine_copy, eng, c, u, half, moved):
            eng.wait_ge(grams, c * UNITS + u + 1)
            if c >= 2 and u == 0:
                eng.wait_ge(dense1, c - 1)
            src = pG[(c * UNITS + u) % 2][:, :].rearrange("m (j n) -> m j n", n=GSTEP)
            at = u * PER_UNIT * PER_GRAM
            for s in (2 * half, 2 * half + 1):
                for r in range(PER_GRAM):
                    n = len(range(r, COLS, PER_GRAM))
                    last = engine_copy(
                        Z[QUAD * r:QUAD * r + COLS, c % 2, FIRST_TILE[r]:FIRST_TILE[r] + n,
                          at + s:at + PER_UNIT * PER_GRAM:PER_GRAM],
                        src[QUAD * s:QUAD * s + COLS, :, COLS * s + r:COLS * s + COLS:PER_GRAM].rearrange("m j t -> m t j"))
            last.then_inc(moved, 1)

        @block.scalar
        def _(act):
            def ids_and_high(n):
                act.wait_ge(ids_spread, n + 1)
                if n >= 2:
                    act.wait_ge(hot_done, (n - 1) * ACT_BLOCK)
                nc.scalar.copy(ids_b[:, n % 2, :],
                               pT[pt_order.index(("ids", n)) % 2][:, 0:B]).then_inc(ids_b_done, 1)
                act.wait_ge(tbl_in[n], 32)
                if n >= 2:
                    act.wait_ge(looked_up, n - 1)
                nc.scalar.copy(high[0:TP, n % 2, :, :], tbl[0:TP, n % TABLE_RING, :, :]).then_inc(high_done, 1)

            def one_hot_block(n):
                act.wait_ge(ids_b_done, n + 1)
                if n:
                    act.wait_ge(hot_act_done, n)
                else:
                    act.wait_ge(row_f_done, 1)
                nc.scalar.activation(away[0:TP, :], ids_b[0:TP, n % 2, :], ACT.Abs, scale=-1.0,
                                     bias=row_f[0:TP, ACT_BLOCK:ACT_BLOCK + 1]).then_inc(away_done, 1)
                act.wait_ge(away_done, n + 1)
                if n >= 2:
                    act.wait_ge(looked_up, n - 1)
                nc.scalar.activation(hot[0:TP, n % 2, ACT_BLOCK, :], away[0:TP, :],
                                     ACT.Relu, scale=-1.0, bias=1.0).then_inc(hot_act_done, 1)

            def move_lookup(n):
                act.wait_ge(looked_up, n + 1)
                nc.scalar.copy(ET[:, :, :, one_hot[n]].rearrange("d c p -> d (c p)"),
                               pG[n % 2][:, 0:B]).then_inc(lookup_moved, 1)

            def zero_pads(c):
                nc.scalar.memzero(ET[:, c, :, FEAT:QUAD]).then_inc(pads_done, 1)

            ids_and_high(0)
            one_hot_block(0)
            for n in range(N_ONE_HOT):
                if n + 1 < N_ONE_HOT:
                    ids_and_high(n + 1)
                    one_hot_block(n + 1)
                if n:
                    move_lookup(n - 1)
                if n >= 2 and (n - 2) % 2 == 1 and n - 2 < EARLY_RUNS:
                    move_run(nc.scalar.copy, act, 0, n - 2)
                for t in range(2 * n, min(2 * n + 2, TILES - STAGED)):
                    nc.scalar.memzero(W1Z[:, t, :]).then_inc(w1z_zeroed, 1)
                if n == 3:
                    zero_pads(0)
            move_lookup(N_ONE_HOT - 1)

            def relu_h1(c):
                act.wait_ge(dense1, c + 1)
                half = K1 // 2
                for k in (0, half):
                    src = pH[:, k * P:(k + half) * P]
                    if c == LAST and k == half:
                        act.wait_ge(dense1, c + 2)
                        src = pH_last[:, 0:half * P]
                    nc.scalar.activation(H1T[:, k:k + half, :].rearrange("n k p -> n (k p)"),
                                         src, ACT.Relu).then_inc(h1_done, 1)

            def runs_of(c, first, end):
                for i in range(first, end):
                    if i % 2 == 1:
                        move_run(nc.scalar.copy, act, c, i)

            runs_of(0, max(N_ONE_HOT - 2, 0), RUNS[0])
            for c in range(CHUNKS):
                if c == 0:
                    act.wait_ge(z_zeroed, 1)
                    act.wait_ge(ones_done, 1)
                for u in range(UNITS):
                    move_gram(nc.scalar.copy, act, c, u, 1, z_act)
                if c + 1 < CHUNKS:
                    zero_pads(c + 1)
                before = RUNS[c + 1] - LATE_RUNS[c + 1] if c < LAST else 0
                runs_of(c + 1, 0, before)
                relu_h1(c)
                if c < LAST:
                    runs_of(c + 1, before, RUNS[c + 1])

        @block.vector
        def _(dve):
            nc.vector.memset(ident[:, :], 0.0).then_inc(ident_zero, 1)
            nc.vector.memset(warm[:, :], 0.0).then_inc(warm_done, 1)
            nc.vector.memset(Z[:, :, :, :], 0.0).then_inc(z_zeroed, 1)
            dve.wait_ge(ident_done, 1)
            nc.vector.tensor_copy(ident_h[:, :], ident[:, :]).then_inc(ident_h_done, 1)
            dve.wait_ge(row_i_done, 1)
            nc.vector.tensor_copy(row_f[:, :], row_i[:, :]).then_inc(row_f_done, 1)
            dve.wait_ge(ids_in, 16)
            ids_cf = ids_sb[:, :].rearrange("p (c f) -> p c f", f=FEAT)
            for n, f in enumerate(one_hot):
                nc.vector.tensor_copy(ids_h[:, n, :], ids_cf[:, :, f]).then_inc(ids_h_done, 1)
            dve.wait_ge(z_zeroed, 1)
            nc.vector.memset(Z[P - QUAD:P, :, TILES - 1, :], 1.0).then_inc(ones_done, 1)
            nc.vector.memset(ones[:, :], 1.0).then_inc(ones_done, 1)
            dve.wait_ge(row_f_done, 1)
            for n in range(N_ONE_HOT):
                dve.wait_ge(ids_b_done, n + 1)
                if n >= 2:
                    dve.wait_ge(looked_up, n - 1)
                for k in range(ACT_BLOCK):
                    if k == TABLE_K // 2:
                        dve.wait_ge(high_done, n + 1)
                        nc.vector.tensor_tensor(low[0:TP, n % 2, :, :], tbl[0:TP, n % TABLE_RING, :, :],
                                                high[0:TP, n % 2, :, :], ALU.subtract).then_inc(low_done, 1)
                    nc.vector.tensor_scalar(hot[0:TP, n % 2, k, :], ids_b[0:TP, n % 2, :],
                                            row_f[0:TP, k:k + 1], None, ALU.is_equal).then_inc(hot_done, 1)
                if n >= 2 and (n - 2) % 2 == 0 and n - 2 < min(EARLY_RUNS, DVE_LATER):
                    move_run(nc.vector.tensor_copy, dve, 0, n - 2)

            def dense3(c):
                dve.wait_ge(dense2, c + 1)
                if c == 0:
                    dve.wait_ge(weights_in, 3 * 16)
                if c:
                    dve.wait_ge(y_done, c)
                h2 = pF
                if c < LAST:
                    nc.vector.tensor_tensor(H2[:, :], pF[:, :], b2_sb[:, :], ALU.add).then_inc(h2_done, 1)
                    dve.wait_ge(h2_done, c + 1)
                    h2 = H2
                nc.vector.scalar_tensor_tensor(out=prod[:, :], in0=h2[:, :], scalar=0.0, in1=W3S[:, :],
                                               op0=ALU.max, op1=ALU.mult, accum_out=y[:, c:c + 1]).then_inc(y_done, 1)

            def runs_of(c, first, end):
                for i in range(first, end):
                    if i % 2 == 0:
                        move_run(nc.vector.tensor_copy, dve, c, i)

            runs_of(0, DVE_LATER, RUNS[0])
            dve.wait_ge(bot_transposed, 1)
            nc.vector.tensor_copy(botT[:, :, :].rearrange("d c p -> d (c p)"), pH[:, :]).then_inc(bot_moved, 1)
            dve.wait_ge(w1ab_in, 32)
            nc.vector.tensor_tensor(W1AB[:, :], W1A[:, :], W1B[:, :], ALU.add).then_inc(w1ab_done, 1)
            for c in range(CHUNKS):
                for u in range(UNITS):
                    move_gram(nc.vector.tensor_copy, dve, c, u, 0, z_dve)
                if c:
                    dense3(c - 1)
                if c + 1 < CHUNKS:
                    runs_of(c + 1, 0, RUNS[c + 1])
            dense3(CHUNKS - 1)

        @block.tensor
        def _(pe):
            def free_pt(use):
                k = pt_order.index(use)
                if k >= 2:
                    before = pt_order[k - 2]
                    if before[0] == "ids":
                        pe.wait_ge(ids_b_done, before[1] + 1)
                    else:
                        pe.wait_ge(mover(before[1]), moved_until(*before))
                return pT[k % 2]

            def spread_ids(n):
                pe.wait_ge(ids_h_done, n + 1)
                bank = free_pt(("ids", n))
                for c in range(CHUNKS):
                    last = nc.tensor.matmul(bank[:, c * P:(c + 1) * P], ids_h[:, n, c:c + 1].to_broadcast([P, P]),
                                            ident_h[:, :], start=True, stop=True)
                last.then_inc(ids_spread, 1)

            def transpose_run(c, i):
                pe.wait_ge(rows_in[c][i], 16 * len(runs[c][i]))
                bank = free_pt((c, i))
                for x, f in enumerate(runs[c][i]):
                    last = nc.tensor.transpose(bank[:, x * P:(x + 1) * P], rows[:, c % 2, slot[f], :], ident[:, :])
                last.then_inc(transposed, 1)

            def dense_layer2(c):
                if 0 < c < LAST:
                    pe.wait_ge(h2_done, c)
                for k in range(K1):
                    if k % (K1 // 2) == 0:
                        pe.wait_ge(h1_done, 2 * c + k // (K1 // 2) + 1)
                    last = nc.tensor.matmul(pF[:, :], H1T[:, k, :], W2S[:, k, :],
                                            start=k == 0 and c < LAST, stop=k == K1 - 1)
                last.then_inc(dense2, 1)

            pe.wait_ge(warm_done, 1)
            for x in range(sum(WARM_UP)):
                if x == WARM_UP[0]:
                    pe.wait_ge(ident_h_done, 1)
                    spread_ids(0)
                    spread_ids(1)
                nc.tensor.matmul(pF[:, 0:P], warm[:, :], warm[:, :], start=True, stop=True)
            for n in range(N_ONE_HOT):
                if n == 1:
                    pe.wait_ge(bot_in, 16)
                    for c in range(CHUNKS):
                        last = nc.tensor.transpose(pH[:, c * P:(c + 1) * P], bot[:, c, :], ident[:, :])
                    last.then_inc(bot_transposed, 1)
                if n >= 2:
                    pe.wait_ge(lookup_moved, n - 1)
                half = TABLE_K // 2
                first, second = range(half), range(half, TABLE_K)
                for x, (part, blocks) in enumerate(((high, first), (low, first), (high, second), (low, second))):
                    if x < 2:
                        pe.wait_ge((high_done, low_done)[x], n + 1)
                    for k in blocks:
                        if part is high and k < ACT_BLOCK:
                            pe.wait_ge(hot_done, n * ACT_BLOCK + k + 1)
                        elif part is high:
                            pe.wait_ge(hot_act_done, n + 1)
                        last = nc.tensor.matmul(pG[n % 2][:, 0:B], part[0:TP, n % 2, k, :],
                                                hot[0:TP, n % 2, k, :],
                                                start=x == 0 and k == 0, stop=x == 3 and k == TABLE_K - 1)
                last.then_inc(looked_up, 1)
                if n + 2 < N_ONE_HOT:
                    spread_ids(n + 2)
                if 0 < n <= EARLY_RUNS:
                    transpose_run(0, n - 1)
            for i in range(EARLY_RUNS, RUNS[0]):
                transpose_run(0, i)

            def dense_layer1(c, weights, acts, units=range(K1), first=False, last=False):
                for k in units:
                    bank, at, clears = pH, k, k == 0
                    if c == LAST and k >= K1 // 2:
                        bank, at, clears = pH_last, k - K1 // 2, k == K1 // 2
                    done = nc.tensor.matmul(bank[:, at * P:(at + 1) * P], weights[:, k * P:(k + 1) * P], acts,
                                            start=first and clears, stop=last, skip_group_check=True)
                return done

            def dense_layer1_bottom(c, units=range(K1)):
                if c:
                    pe.wait_ge(h1_done, 2 * c)
                else:
                    pe.wait_ge(bot_moved, 1)
                    pe.wait_ge(w1ab_done, 1)
                if c == LAST and K1 - 1 in units:
                    pe.wait_ge(mover(spare_use[1]), moved_until(*spare_use))
                dense_layer1(c, W1AB, botT[:, c, :], units, first=True)

            for c in range(CHUNKS):
                if c == CHUNKS - 1:
                    dense_layer1_bottom(c, range(K1 // 2))
                pe.wait_ge(pads_done, c + 1)
                for i in range(max(RUNS[c] - 2, 0), RUNS[c]):
                    pe.wait_ge(mover(i), moved_until(c, i))
                for u in range(UNITS):
                    k = c * UNITS + u
                    if k == 0:
                        pe.wait_ge(lookup_moved, N_ONE_HOT)
                    if k >= 2:
                        pe.wait_ge(z_dve, k - 1)
                        pe.wait_ge(z_act, k - 1)
                    for j in range(PER_UNIT):
                        s0 = PER_GRAM * (u * PER_UNIT + j)
                        four = ET[:, c, s0:s0 + PER_GRAM, :]
                        last = nc.tensor.matmul(pG[k % 2][0:GRAM_ROWS, j * GSTEP:j * GSTEP + PER_GRAM * COLS],
                                                four.rearrange("d s f -> d (s f)")[:, 0:GRAM_ROWS], four[:, :, 1:FEAT],
                                                start=True, stop=True)
                    last.then_inc(grams, 1)
                early = list(range(RUNS[c + 1] - LATE_RUNS[c + 1])) if c < LAST else []

                def next_run():
                    if early:
                        transpose_run(c + 1, early.pop(0))

                next_run()
                if c:
                    dense_layer2(c - 1)
                if c + 1 < LAST:
                    next_run()
                dense_layer1_bottom(c, range(K1 // 2, K1) if c == LAST else range(K1))
                next_run()
                if c == 0:
                    pe.wait_ge(weights_in, 3 * 16)
                    pe.wait_ge(ones_done, 1)
                    pe.wait_ge(w1z_in, 16 * (COLS + 1))
                pe.wait_ge(z_dve, (c + 1) * UNITS)
                pe.wait_ge(z_act, (c + 1) * UNITS)

                def pairs(t, units=range(K1), last=False):
                    return dense_layer1(c, W1Z[:, t - STAGED, :], Z[:, c % 2, t, :], units, last=last)

                for t in range(2 * STAGED, TILES):
                    pairs(t)
                    next_run()
                if c == 0:
                    next_run()
                if c == LAST:
                    pe.wait_ge(ones_done, 2)
                    pe.wait_ge(h2_done, c)
                    nc.tensor.matmul(pF[:, :], ones[0:1, :], b2_sb[0:1, :], start=True, stop=False)
                pe.wait_ge(packed_long, 16 * (LONG * (c + 1) - (c == LAST)))
                if c == LAST:
                    pe.wait_ge(packed_pool, 16)
                pairs(STAGED)
                next_run()
                pe.wait_ge(packed_short, 16 * (PER_GRAM - LONG) * (c + 1))
                end_tiles = range(STAGED + 1, 2 * STAGED)
                for units in ((range(K1 // 2), range(K1 // 2, K1)) if c == LAST else (range(K1),)):
                    for t in end_tiles:
                        done = pairs(t, units, last=t == end_tiles[-1])
                        if t != end_tiles[-1]:
                            next_run()
                    done.then_inc(dense1, 1)
                if c < LAST:
                    for i in range(RUNS[c + 1] - LATE_RUNS[c + 1], RUNS[c + 1]):
                        transpose_run(c + 1, i)
            dense_layer2(LAST)


def kernel(**inputs):
    import numpy as np
    import concourse.bacc as bacc
    from concourse.bass_utils import run_bass_kernel_spmd

    n_tables = sum(name.startswith("tbl_") for name in inputs)
    names = ["r_bottom_mlp_out", "ids"] + [f"tbl_{i}" for i in range(n_tables)] + ["W_top1", "b_top1", "W_top2", "b_top2", "W_top3"]
    nc = bacc.Bacc("TRN2", target_bir_lowering=False, num_devices=1)
    arrays, aps = {}, {}
    for name in names:
        a = np.ascontiguousarray(inputs[name])
        arrays[f"in_{name}"] = a
        aps[name] = nc.dram_tensor(f"in_{name}", a.shape, mybir.dt.from_np(a.dtype), kind="ExternalInput").ap()
    out = nc.dram_tensor("out_y", (inputs["ids"].shape[0], 1), F32, kind="ExternalOutput").ap()
    dlrm_tower_kernel(nc, aps["r_bottom_mlp_out"], aps["ids"], [aps[f"tbl_{i}"] for i in range(n_tables)],
                      aps["W_top1"], aps["b_top1"], aps["W_top2"], aps["b_top2"], aps["W_top3"], out)
    r = run_bass_kernel_spmd(nc, [arrays], core_ids=[0])
    return r.results[0]["out_y"]
```
